# Optimizing a Trainium2 kernel written in Bass

```python
import numpy as np
import jax
import jax.numpy as jnp

def _softmax(x, axis=-1):
    return jax.nn.softmax(x, axis=axis)

def _gelu(x):
    return jax.nn.gelu(x, approximate=True)

def _silu(x):
    return jax.nn.silu(x)

def _sigmoid(x):
    return jax.nn.sigmoid(x)

def _layernorm(x, axis=-1, eps=1e-05):
    m = jnp.mean(x, axis=axis, keepdims=True)
    v = jnp.var(x, axis=axis, keepdims=True)
    return (x - m) / jnp.sqrt(v + eps)

def _scatter_add(tgt, idx, src, axis=0):
    return tgt.at[idx].add(src)

def _segment_sum(src, seg, n):
    return jax.ops.segment_sum(src, seg, n)
kernel_name = 'mk_macaron_d1_jaxref_r8_d16586'

def setup_inputs(seed: int=0):
    np.random.seed(seed)
    _w = jnp.asarray

    def _L0_attn_setup():
        import jax, jax.numpy as jnp
        import numpy as np
        EMBED_DIM = 128
        NUM_HEADS = 16
        HEAD_DIM = EMBED_DIM // NUM_HEADS
        WL_CHANNELS = 16
        BATCH = 1
        SEQ = 128
        KERR = 2.7e-18 * 1000000.0
        SCALE = 1.0 / np.sqrt(HEAD_DIM)
        W_INIT = 0.02
        key = jax.random.key(seed)
        ks = jax.random.split(key, 7)
        x = jax.random.normal(ks[0], (BATCH, SEQ, EMBED_DIM), dtype=jnp.float32)
        Wq = jax.random.normal(ks[1], (EMBED_DIM, EMBED_DIM), dtype=jnp.float32) * W_INIT
        Wk = jax.random.normal(ks[2], (EMBED_DIM, EMBED_DIM), dtype=jnp.float32) * W_INIT
        Wv = jax.random.normal(ks[3], (EMBED_DIM, EMBED_DIM), dtype=jnp.float32) * W_INIT
        Wo = jax.random.normal(ks[4], (EMBED_DIM, EMBED_DIM), dtype=jnp.float32) * W_INIT
        bq = jnp.zeros((EMBED_DIM,), jnp.float32)
        bk = jnp.zeros((EMBED_DIM,), jnp.float32)
        bv = jnp.zeros((EMBED_DIM,), jnp.float32)
        bo = jnp.zeros((EMBED_DIM,), jnp.float32)
        phase_modulators = jax.random.normal(ks[5], (WL_CHANNELS, NUM_HEADS), dtype=jnp.float32)
        interference_weights = jnp.ones((WL_CHANNELS,), jnp.float32)
        return {'x': x, 'Wq': Wq, 'bq': bq, 'Wk': Wk, 'bk': bk, 'Wv': Wv, 'bv': bv, 'Wo': Wo, 'bo': bo, 'phase_modulators': phase_modulators, 'interference_weights': interference_weights}
    _L0_attn_in = _L0_attn_setup()

    def _L0_ffn_setup():
        import jax, jax.numpy as jnp
        import numpy as np
        B, S, DIM = (4, 256, 128)
        E, K, HID = (8, 2, 512)
        key = jax.random.key(seed)
        ks = jax.random.split(key, 8)
        init = lambda k, sh: jax.random.normal(k, sh, jnp.float32) * 0.02
        return {'x': jax.random.normal(ks[0], (B, S, DIM), jnp.float32), 'gate_w': init(ks[1], (DIM, E)), 'gate_b': jnp.zeros((E,), jnp.float32), 'w1': init(ks[2], (E, DIM, HID)), 'b1': jnp.zeros((E, HID), jnp.float32), 'w2': init(ks[3], (E, HID, DIM)), 'b2': jnp.zeros((E, DIM), jnp.float32), 'ws1': init(ks[4], (DIM, HID)), 'bs1': jnp.zeros((HID,), jnp.float32), 'ws2': init(ks[5], (HID, DIM)), 'bs2': jnp.zeros((DIM,), jnp.float32)}
    _L0_ffn_in = _L0_ffn_setup()
    _d = {'L0_attn_x': _L0_attn_in['x'], 'L0_attn_Wq': _L0_attn_in['Wq'], 'L0_attn_bq': _L0_attn_in['bq'], 'L0_attn_Wk': _L0_attn_in['Wk'], 'L0_attn_bk': _L0_attn_in['bk'], 'L0_attn_Wv': _L0_attn_in['Wv'], 'L0_attn_bv': _L0_attn_in['bv'], 'L0_attn_Wo': _L0_attn_in['Wo'], 'L0_attn_bo': _L0_attn_in['bo'], 'L0_attn_phase_modulators': _L0_attn_in['phase_modulators'], 'L0_attn_interference_weights': _L0_attn_in['interference_weights'], 'L0_ffn_gate_w': _L0_ffn_in['gate_w'], 'L0_ffn_gate_b': _L0_ffn_in['gate_b'], 'L0_ffn_w1': _L0_ffn_in['w1'], 'L0_ffn_b1': _L0_ffn_in['b1'], 'L0_ffn_w2': _L0_ffn_in['w2'], 'L0_ffn_b2': _L0_ffn_in['b2'], 'L0_ffn_ws1': _L0_ffn_in['ws1'], 'L0_ffn_bs1': _L0_ffn_in['bs1'], 'L0_ffn_ws2': _L0_ffn_in['ws2'], 'L0_ffn_bs2': _L0_ffn_in['bs2']}
    _x0 = _d['L0_attn_x']
    _d['L0_attn_x'] = jax.random.normal(jax.random.fold_in(jax.random.key(seed), 1), (16, 256, 128), dtype=_x0.dtype)
    del _x0
    return _d

def reference(L0_attn_x, L0_attn_Wq, L0_attn_bq, L0_attn_Wk, L0_attn_bk, L0_attn_Wv, L0_attn_bv, L0_attn_Wo, L0_attn_bo, L0_attn_phase_modulators, L0_attn_interference_weights, L0_ffn_gate_w, L0_ffn_gate_b, L0_ffn_w1, L0_ffn_b1, L0_ffn_w2, L0_ffn_b2, L0_ffn_ws1, L0_ffn_bs1, L0_ffn_ws2, L0_ffn_bs2):

    def _L0_attn_ref(x, Wq, bq, Wk, bk, Wv, bv, Wo, bo, phase_modulators, interference_weights):
        import jax, jax.numpy as jnp
        import numpy as np
        EMBED_DIM = 128
        NUM_HEADS = 16
        HEAD_DIM = EMBED_DIM // NUM_HEADS
        WL_CHANNELS = 16
        BATCH = 1
        SEQ = 128
        KERR = 2.7e-18 * 1000000.0
        SCALE = 1.0 / np.sqrt(HEAD_DIM)
        W_INIT = 0.02
        B, S, E = x.shape
        H, D = (NUM_HEADS, HEAD_DIM)

        def proj(W, b):
            y = jnp.einsum('bse,ef->bsf', x, W) + b
            return y.reshape(B, S, H, D).transpose(0, 2, 1, 3)
        Q = proj(Wq, bq)
        K = proj(Wk, bk)
        V = proj(Wv, bv)
        cos_pm = jnp.cos(phase_modulators)

        def wl_step(acc, wl):
            cpm, iw = wl
            m = cpm[None, :, None, None]
            Qw = Q * m
            Kw = K * m
            scores = jnp.einsum('bhqd,bhkd->bhqk', Qw, Kw) * SCALE
            scores = scores * jnp.cos(KERR * scores * scores)
            attn = jax.nn.softmax(scores, axis=-1)
            out = jnp.einsum('bhqk,bhkd->bhqd', attn, V)
            return (acc + out * iw, None)
        acc0 = jnp.zeros((B, H, S, D), x.dtype)
        acc, _ = jax.lax.scan(wl_step, acc0, (cos_pm, interference_weights))
        combined = acc / WL_CHANNELS
        combined = combined.transpose(0, 2, 1, 3).reshape(B, S, E)
        return jnp.einsum('bse,ef->bsf', combined, Wo) + bo

    def _L0_ffn_ref(x, gate_w, gate_b, w1, b1, w2, b2, ws1, bs1, ws2, bs2):
        import jax, jax.numpy as jnp
        import numpy as np
        B, S, DIM = (4, 256, 128)
        E, K, HID = (8, 2, 512)
        orig_shape = x.shape
        xf = x.reshape(-1, DIM)
        logits = xf @ gate_w + gate_b
        top_w, top_i = jax.lax.top_k(logits, K)
        gw = jax.nn.softmax(top_w, axis=-1).astype(xf.dtype)
        combine = (gw[:, :, None] * jax.nn.one_hot(top_i, E, dtype=xf.dtype)).sum(axis=1)
        out = jnp.zeros_like(xf)
        for e in range(E):
            h = jax.nn.gelu(xf @ w1[e] + b1[e], approximate=False)
            out = out + combine[:, e:e + 1] * (h @ w2[e] + b2[e])
        shared = jax.nn.gelu(xf @ ws1 + bs1, approximate=False) @ ws2 + bs2
        return (out + shared).reshape(orig_shape)
    x = L0_attn_x
    x = x + 0.5 * _L0_ffn_ref(_layernorm(x, axis=-1), L0_ffn_gate_w, L0_ffn_gate_b, L0_ffn_w1, L0_ffn_b1, L0_ffn_w2, L0_ffn_b2, L0_ffn_ws1, L0_ffn_bs1, L0_ffn_ws2, L0_ffn_bs2)
    x = x + _L0_attn_ref(_layernorm(x, axis=-1), L0_attn_Wq, L0_attn_bq, L0_attn_Wk, L0_attn_bk, L0_attn_Wv, L0_attn_bv, L0_attn_Wo, L0_attn_bo, L0_attn_phase_modulators, L0_attn_interference_weights)
    x = x + 0.5 * _L0_ffn_ref(_layernorm(x, axis=-1), L0_ffn_gate_w, L0_ffn_gate_b, L0_ffn_w1, L0_ffn_b1, L0_ffn_w2, L0_ffn_b2, L0_ffn_ws1, L0_ffn_bs1, L0_ffn_ws2, L0_ffn_bs2)
    return x

_drawn_inputs = setup_inputs


def setup_inputs(seed=0):
    import zlib

    import numpy as np

    out = dict(_drawn_inputs(seed))
    spreads = {'L0_attn_bq': (0.0, 0.8),
     'L0_attn_bk': (0.0, 0.8),
     'L0_attn_bv': (0.0, 0.363),
     'L0_attn_bo': (0.0, 0.1),
     'L0_attn_interference_weights': (1.0, 0.6),
     'L0_ffn_gate_b': (0.0, 0.1),
     'L0_ffn_b1': (0.0, 0.481),
     'L0_ffn_b2': (0.0, 0.1),
     'L0_ffn_bs1': (0.0, 0.366),
     'L0_ffn_bs2': (0.0, 0.1)}
    factors = {'L0_attn_Wq': 8.0,
     'L0_attn_Wk': 8.0,
     'L0_attn_Wv': 8.0,
     'L0_attn_Wo': 2.805,
     'L0_attn_phase_modulators': 8.0}
    for name, (base, spread) in spreads.items():
        noise = np.random.default_rng([zlib.crc32(name.encode()), seed]).standard_normal(out[name].shape)
        drawn = base * np.exp(spread * noise) if base else spread * noise
        out[name] = jnp.asarray(drawn.astype(out[name].dtype))
    for name, factor in factors.items():
        out[name] = (out[name] * factor).astype(out[name].dtype)
    return out
```

```python
from contextlib import ExitStack

import numpy as np

import concourse.bass as bass
import concourse.mybir as mybir

F32 = mybir.dt.float32
F32R = mybir.dt.float32r
U32 = mybir.dt.uint32
ALU = mybir.AluOpType
ACT = mybir.ActivationFunctionType
AX = mybir.AxisListType.X

P = 128
B, S, D = 16, 256, 128
H, HD, W = 16, 8, 16
E, HID = 8, 512
NE = E + 1
HC = HID // P
J = 4
G = B // J
R = S // 32
T = G * R
GT = R * P
TB = 512
NTB = B * S // TB
EPS = 1e-5
KERR = 2.7e-18 * 1000000.0
COS_IS_ONE = 1e-4
PI_BELOW = 3.1415925
SCALE = float(1.0 / np.sqrt(HD))
MAGIC = float(1.5 * 2 ** 23)
TWO_PI_A = 6.28125
TWO_PI_B = float(np.float32(np.round((2 * np.pi - TWO_PI_A) * 2 ** 20) / 2 ** 20))
TWO_PI_C = float(np.float32(2 * np.pi - TWO_PI_A - TWO_PI_B))


class Steps:

    def __init__(self, eng, sem):
        self.eng, self.sem, self.base, self.n = eng, sem, 0, 0

    def did(self, instruction):
        instruction.then_inc(self.sem, 1)
        self.n += 1

    def wait(self):
        self.eng.wait_ge(self.sem, self.base + self.n)

    def loop(self, base):
        self.base, self.n = base, 0


def wait_alone(eng, sem, value, passed):
    eng.wait_ge(sem, value)
    eng.sem_inc(passed, 1)


def setup_block(nc, c, d):
    with ExitStack() as ctx:
        sem = lambda name: ctx.enter_context(nc.semaphore(name))
        small_loaded, pool_step, dve_step, rows_ready, cols_done, sin_ready = map(
            sem, ("small_loaded", "pool_step", "setup_dve_step", "rows_ready", "cols_done", "sin_ready"))
        zeros_done, angle_ready = sem("zeros_done"), sem("angle_ready")
        sb = lambda name, shape, dt=F32: ctx.enter_context(nc.sbuf_tensor(name, shape, dt))
        pm = sb("pm", [P, W * H])
        turns = sb("turns", [P, W * H])
        half_sin = sb("half_sin", [P, W * H])
        bias_in = sb("bias_in", [1, 2, D])
        rows = sb("rows", [1, 10, P])
        one = sb("one", [1, 1])
        sel = sb("sel", [16, E, P])
        minus = sb("minus_in", [P, P])
        iw_in = sb("iw_in", [P, W])
        wqk = sb("setup_wqk", [P, 2, D])
        squares = sb("squares", [P, 2, D])
        ones = sb("ones", [P, 1])
        reach = sb("reach", [1, 2, D])
        bias_sq = sb("bias_sq", [1, 2, D])
        by_head = sb("by_head", [1, 2, H])
        squares_ready, sums_done = sem("squares_ready"), sem("sums_done")
        N_LOADS = 9
        block = ctx.enter_context(nc.Block())

        @block.sync
        def _(sp):
            for t in range(4):
                sp.dma_start(pm[32 * t:32 * t + 32, :],
                             d["pm"].rearrange("w h -> (w h)").partition_broadcast(32)).then_inc(small_loaded, 16)
            sp.dma_start(wqk[:, 0, :], d["wq"]).then_inc(small_loaded, 16)
            sp.dma_start(wqk[:, 1, :], d["wk"]).then_inc(small_loaded, 16)
            sp.dma_start(iw_in[:, :], d["iw"].partition_broadcast(P)).then_inc(small_loaded, 16)
            sp.dma_start(bias_in[0:1, 0, :], d["bq"].rearrange("(a n) -> a n", a=1)).then_inc(small_loaded, 16)
            sp.dma_start(bias_in[0:1, 1, :], d["bk"].rearrange("(a n) -> a n", a=1)).then_inc(small_loaded, 16)

        @block.scalar
        def _(act):
            for g in range(G):
                for j in range(J):
                    act.dma_start(c["x"][32 * j:32 * j + 32, g * R:g * R + R, :],
                                  d["x"][J * g + j].rearrange("(r p) d -> p r d", p=32)).then_inc(c["x_loaded"], 16)
            act.wait_ge(angle_ready, 2)
            nc.scalar.activation(half_sin[:, :], turns[:, :], ACT.Sin, scale=0.5).then_inc(sin_ready, 1)

        @block.gpsimd
        def _(pool):
            step = Steps(pool, pool_step)
            step.did(nc.gpsimd.memset(c["ident"][:, :], 0.0))
            step.did(nc.gpsimd.memset(sel[:, :, :], 0.0))
            step.did(nc.gpsimd.memset(minus[:, :], -1.0))
            step.wait()
            step.did(nc.gpsimd.affine_select(out=c["ident"][:, :], in_=c["ident"][:, :],
                                             compare_op=ALU.not_equal, fill=1.0, base=0,
                                             pattern=[[-1, P]], channel_multiplier=1))
            for base in (0, -E):
                step.did(nc.gpsimd.affine_select(out=sel[:, :, :], in_=sel[:, :, :],
                                                 compare_op=ALU.not_equal, fill=1.0, base=base,
                                                 pattern=[[-1, E], [0, P]], channel_multiplier=1))
                step.wait()
            nc.gpsimd.iota(c["iota"][:, :], pattern=[[1, E]], base=0, channel_multiplier=0).then_inc(zeros_done, 1)

        @block.vector
        def _(dve):
            step = Steps(dve, dve_step)
            step.did(nc.vector.memset(one[:, :], 1.0))
            step.did(nc.vector.memset(rows[:, 8:10, :], 0.0))
            step.wait()
            mask = lambda n: rows[0:1, n, :].rearrange("a (i c d) -> a i c d", c=4, d=HD)
            for n, copy in ((8, 1), (8, 3), (9, 2), (9, 3)):
                step.did(nc.vector.memset(mask(n)[:, :, copy, :], -1.0))
            dve.wait_ge(small_loaded, 16 * N_LOADS)
            for n in range(2):
                for hq in range(4):
                    step.did(nc.vector.tensor_copy(
                        rows[0:1, 2 * hq + n, :].rearrange("a (i c d) -> a i c d", c=4, d=HD),
                        bias_in[0:1, n, 32 * hq:32 * hq + 32].rearrange("a (i d) -> a i d", d=HD)
                        .unsqueeze(2).to_broadcast([1, 4, 4, HD])))
            step.wait()
            nc.vector.tensor_copy(one[:, :], one[:, :]).then_inc(rows_ready, 1)
            step.did(nc.vector.memset(ones[:, :], 1.0))
            nc.vector.tensor_tensor(squares[:, :, :], wqk[:, :, :], wqk[:, :, :], ALU.mult).then_inc(squares_ready, 1)
            step.wait()
            nc.vector.tensor_copy(ones[:, :], ones[:, :]).then_inc(squares_ready, 1)
            nc.vector.tensor_scalar(c["iw"][:, :], iw_in[:, :], 1.0 / W, None, ALU.mult).then_inc(angle_ready, 1)
            step.did(nc.vector.tensor_scalar(turns[:, :], pm[:, :], float(1 / (2 * np.pi)), MAGIC, ALU.mult, ALU.add))
            step.wait()
            step.did(nc.vector.tensor_scalar(turns[:, :], turns[:, :], -MAGIC, None, ALU.add))
            for part in (TWO_PI_A, TWO_PI_B, TWO_PI_C):
                step.wait()
                step.did(nc.vector.scalar_tensor_tensor(out=pm[:, :], in0=turns[:, :], scalar=-part,
                                                        in1=pm[:, :], op0=ALU.mult, op1=ALU.add))
            step.wait()
            nc.vector.tensor_copy(turns[:, :], pm[:, :]).then_inc(angle_ready, 1)
            dve.wait_ge(sin_ready, 1)
            step.did(nc.vector.tensor_tensor(half_sin[:, :], half_sin[:, :], half_sin[:, :], ALU.mult))
            step.wait()
            step.did(nc.vector.tensor_scalar(half_sin[:, :], half_sin[:, :], -2.0, 1.0, ALU.mult, ALU.add))
            step.wait()
            step.did(nc.vector.tensor_tensor(half_sin[:, :], half_sin[:, :], half_sin[:, :], ALU.mult))
            step.wait()
            step.did(nc.vector.tensor_scalar(c["gain"][:, :].rearrange("p (h w) -> p w h", w=W),
                                             half_sin[:, :].rearrange("p (w h) -> p w h", h=H),
                                             SCALE, None, ALU.mult))
            step.did(nc.vector.tensor_tensor(bias_sq[:, :, :], bias_in[:, :, :], bias_in[:, :, :], ALU.mult))
            step.wait()
            dve.wait_ge(sums_done, 1)
            step.did(nc.vector.scalar_tensor_tensor(
                out=reach[:, :, :].rearrange("p a n -> p (a n)"), in0=c["bank"][1][0:1, 0:2 * D], scalar=float(D),
                in1=bias_sq[:, :, :].rearrange("p a n -> p (a n)"), op0=ALU.mult, op1=ALU.add))
            step.wait()
            step.did(nc.vector.reduce_sum(by_head[:, :, :], reach[:, :, :].rearrange("p a (h d) -> p a h d", d=HD),
                                          axis=AX))
            step.wait()
            step.did(nc.vector.tensor_tensor(by_head[:, 0, :], by_head[:, 0, :], by_head[:, 1, :], ALU.mult))
            step.wait()
            step.did(nc.vector.reduce_max(reach[:, 0, 0:1], by_head[:, 0, :], axis=AX))
            step.wait()
            step.did(nc.vector.tensor_scalar(reach[:, 0, 1:2], reach[:, 0, 0:1], 4 * KERR * SCALE * SCALE, COS_IS_ONE,
                                             ALU.mult, ALU.is_lt))
            step.wait()
            step.did(nc.vector.tensor_copy(c["bounded"][:, :], reach[:, 0, 1:2]))
            dve.wait_ge(cols_done, 10)
            step.did(nc.vector.tensor_copy(c["cols"][:, :], c["bank"][0][:, 0:10]))
            dve.wait_ge(pool_step, 6)
            step.did(nc.vector.tensor_copy(c["sel"][:, :, :], sel[:, :, :]))
            step.did(nc.vector.tensor_copy(c["minus"][:, :], minus[:, :]))
            dve.wait_ge(zeros_done, 1)
            step.did(nc.vector.tensor_copy(c["iotaf"][:, :], c["iota"][:, :]))
            step.wait()

        @block.tensor
        def _(pe):
            pe.wait_ge(squares_ready, 2)
            nc.tensor.matmul(c["bank"][1][0:1, 0:2 * D], ones[:, :], squares[:, :, :].rearrange("p a n -> p (a n)"),
                             start=True, stop=True).then_inc(sums_done, 1)
            pe.wait_ge(rows_ready, 1)
            for n in range(10):
                nc.tensor.matmul(c["bank"][0][:, n:n + 1], rows[0:1, n, :], one[0:1, 0:1],
                                 start=True, stop=True).then_inc(cols_done, 1)



def norm_block(nc, c, name, loads, xT_view, loaded=None, gate=None, low=None, beside=None, also=None):
    x = c["x"]
    with ExitStack() as ctx:
        sem = lambda n: ctx.enter_context(nc.semaphore(f"{name}_{n}"))
        sb = lambda n, shape, dt=F32: ctx.enter_context(nc.sbuf_tensor(f"{name}_{n}", shape, dt))
        (dve_step, centred, squared, var_ready, sqrt_done, xn_ready, xT_psum, xT_sb, xT_copied, logits_done,
         low_done) = map(
            sem, ("dve_step", "centred", "squared", "var_ready", "sqrt_done", "xn_ready", "xT_psum", "xT_sb",
                  "xT_copied", "logits_done", "low_done"))
        top_ready, index_ready, gap_ready, gap_exp, weights_split, cT_psum, cT_free, gate_loaded, passed = map(
            sem, ("top_ready", "index_ready", "gap_ready", "gap_exp", "weights_split", "cT_psum", "cT_free",
                  "gate_loaded", "passed"))
        xn = [sb(f"xn{n}", [P, R, D]) for n in range(2)]
        xTc = [sb(f"xTc{n}", [P, GT]) for n in range(2)]
        sums, var, std, rstd, tmp = (sb(n, [P, T]) for n in ("sums", "var", "std", "rstd", "tmp"))
        bank = c["bank"]
        if gate:
            GT2 = 2 * R
            logits = sb("logits", [P, GT2, E])
            top8 = sb("top8", [P, GT2, 8])
            idx8 = sb("idx8", [P, GT2, 8], U32)
            top = sb("top", [P, T, 2])
            idxf = sb("idxf", [P, T, 2])
            gap, w1, w2 = (sb(n, [P, T]) for n in ("gap", "w1", "w2"))
            first, second = sb("first", [P, T, E]), sb("second", [P, T, E])
            parts = sb("parts", [P, T, 2 * E], F32R)
            gw, gb = sb("gw", [P, E]), sb("gb", [P, E])
            ident = sb("ident", [P, P], F32R)
        tiles = lambda g: x[:, g * R:g * R + R, :]
        block = ctx.enter_context(nc.Block())

        @block.sync
        def _(sp):
            if gate:
                sp.dma_start(gw[:, :], gate["gate_w"]).then_inc(gate_loaded, 16)
                sp.dma_start(gb[:, :], gate["gate_b"].partition_broadcast(P)).then_inc(gate_loaded, 16)
            loads(sp)

        if beside:
            block.gpsimd(beside)

        @block.vector
        def _(dve):
            step = Steps(dve, dve_step)
            if loaded is not None:
                dve.wait_ge(loaded, 16 * B)
            step.did(nc.vector.reduce_sum(sums[:, :], x[:, :, :], axis=AX))
            step.wait()
            step.did(nc.vector.tensor_scalar(sums[:, :], sums[:, :], -1.0 / D, None, ALU.mult))
            step.wait()

            def centre(g):
                return nc.vector.tensor_tensor(
                    xn[g % 2][:, :, :], tiles(g),
                    sums[:, g * R:g * R + R].unsqueeze(2).to_broadcast([P, R, D]), ALU.add)

            for g in range(G + 1):
                if g < G:
                    if g >= 2:
                        dve.wait_ge(var_ready, g - 1)
                    centre(g).then_inc(centred, 1)
                if g:
                    dve.wait_ge(squared, g)
                    nc.vector.reduce_sum(var[:, (g - 1) * R:g * R], xn[(g - 1) % 2][:, :, :], axis=AX)\
                        .then_inc(var_ready, 1)
            dve.wait_ge(var_ready, G)
            nc.vector.tensor_scalar(var[:, :], var[:, :], 1.0 / D, EPS, ALU.mult, ALU.add).then_inc(var_ready, 1)
            dve.wait_ge(sqrt_done, 1)
            step.did(nc.vector.reciprocal(rstd[:, :], std[:, :]))
            step.wait()
            step.did(nc.vector.tensor_tensor(tmp[:, :], rstd[:, :], rstd[:, :], ALU.mult))
            step.wait()
            step.did(nc.vector.tensor_tensor(tmp[:, :], tmp[:, :], var[:, :], ALU.mult))
            step.wait()
            step.did(nc.vector.tensor_scalar(tmp[:, :], tmp[:, :], -0.5, 1.5, ALU.mult, ALU.add))
            step.wait()
            step.did(nc.vector.tensor_tensor(rstd[:, :], rstd[:, :], tmp[:, :], ALU.mult))
            step.wait()

            def normalise(g):
                if g >= 2:
                    dve.wait_ge(xT_psum, 2 * (g - 1))
                step.did(centre(g))
                step.wait()
                nc.vector.tensor_tensor(xn[g % 2][:, :, :], xn[g % 2][:, :, :],
                                        rstd[:, g * R:g * R + R].unsqueeze(2).to_broadcast([P, R, D]),
                                        ALU.mult).then_inc(xn_ready, 1)

            def transposed(g):
                if g >= 2:
                    dve.wait_ge(xT_copied, g - 1)
                    if low:
                        dve.wait_ge(low_done, g - 1)
                    if gate:
                        dve.wait_ge(logits_done, g - 1)
                for half in range(2):
                    dve.wait_ge(xT_psum, 2 * g + 1 + half)
                    nc.vector.tensor_copy(xTc[g % 2][:, half * 512:half * 512 + 512],
                                          bank[g % 2 * 2 + half][:, :]).then_inc(xT_sb, 1)

            def low_part(g):
                high, rest = low(g)
                dve.wait_ge(xT_copied, g + 1)
                dve.wait_ge(xT_sb, g * 2 + 2)
                nc.vector.tensor_tensor(rest, xTc[g % 2][:, :], high.bitcast(F32), ALU.subtract)\
                    .then_inc(low_done, 1)

            normalise(0)
            for g in range(G + 1):
                if g + 1 < G:
                    normalise(g + 1)
                if g < G:
                    transposed(g)
                if g and low:
                    low_part(g - 1)
            if gate:
                dve.wait_ge(logits_done, G)
                before = step.n
                with dve.Fori(0, T // GT2) as n:
                    step.loop(n * 3 + before)
                    step.did(nc.vector.tensor_tensor(
                        logits[:, :, :],
                        bank[4][:, bass.ds(n * (GT2 * E), GT2 * E)].rearrange("p (t e) -> p t e", e=E),
                        gb[:, :].unsqueeze(1).to_broadcast([P, GT2, E]), ALU.add))
                    wait_alone(dve, dve_step, step.base + step.n, passed)
                    for t in range(GT2):
                        nc.vector.max(top8[:, t, :], logits[:, t, :]).then_inc(top_ready, 1)
                    wait_alone(dve, top_ready, n * GT2 + GT2, passed)
                    for t in range(GT2):
                        nc.vector.max_index(idx8[:, t, :], top8[:, t, :], logits[:, t, :]).then_inc(index_ready, 1)
                    dve.wait_ge(index_ready, n * GT2 + GT2)
                    step.did(nc.vector.tensor_copy(top[:, bass.ds(n * GT2, GT2), :], top8[:, :, 0:2]))
                    step.did(nc.vector.tensor_copy(idxf[:, bass.ds(n * GT2, GT2), :], idx8[:, :, 0:2]))
                step.loop(T // GT2 * 3 + before)
                step.wait()
                nc.vector.tensor_tensor(gap[:, :], top[:, :, 1], top[:, :, 0], ALU.subtract).then_inc(gap_ready, 1)
                dve.wait_ge(gap_exp, 1)
                step.did(nc.vector.tensor_scalar(w1[:, :], gap[:, :], 1.0, None, ALU.add))
                step.wait()
                step.did(nc.vector.reciprocal(w1[:, :], w1[:, :]))
                step.wait()
                step.did(nc.vector.tensor_tensor(w2[:, :], w1[:, :], gap[:, :], ALU.mult))
                wide = lambda a: a.unsqueeze(2).to_broadcast([P, T, E])
                iota = c["iotaf"][:, :].unsqueeze(1).to_broadcast([P, T, E])
                step.did(nc.vector.tensor_tensor(first[:, :, :], iota, wide(idxf[:, :, 0]), ALU.is_equal))
                step.did(nc.vector.tensor_tensor(second[:, :, :], iota, wide(idxf[:, :, 1]), ALU.is_equal))
                step.wait()
                step.did(nc.vector.tensor_tensor(first[:, :, :], first[:, :, :], wide(w1[:, :]), ALU.mult))
                step.did(nc.vector.tensor_tensor(second[:, :, :], second[:, :, :], wide(w2[:, :]), ALU.mult))
                step.wait()
                step.did(nc.vector.tensor_tensor(first[:, :, :], first[:, :, :], second[:, :, :], ALU.add))
                step.wait()
                nc.vector.tensor_copy(ident[:, :], c["ident"][:, :]).then_inc(weights_split, 1)
                nc.vector.tensor_copy(parts[:, :, 0:E], first[:, :, :]).then_inc(weights_split, 1)
                dve.wait_ge(weights_split, 2)
                nc.vector.tensor_tensor(parts[:, :, E:2 * E], first[:, :, :], parts[:, :, 0:E].bitcast(F32),
                                        ALU.subtract).then_inc(weights_split, 1)
                for n in range(T // 4):
                    dve.wait_ge(cT_psum, 4 * n + 4)
                    nc.vector.tensor_copy(gate["weightsT"][:, n * 512:n * 512 + 512],
                                          bank[n % 4][0:16, :]).then_inc(cT_free, 1)

        @block.scalar
        def _(act):
            for g in range(G):
                act.wait_ge(centred, g + 1)
                nc.scalar.activation(xn[g % 2][:, :, :], xn[g % 2][:, :, :], ACT.Square).then_inc(squared, 1)
            act.wait_ge(var_ready, G + 1)
            nc.scalar.activation(std[:, :], var[:, :], ACT.Sqrt).then_inc(sqrt_done, 1)
            if also:
                also(act, 0)
            for g in range(G):
                act.wait_ge(xT_sb, g * 2 + 2)
                for half in range(2):
                    out, view = xT_view(g, half)
                    last = nc.scalar.activation(out, view(xTc[g % 2][:, half * 512:half * 512 + 512]), ACT.Copy)
                last.then_inc(xT_copied, 1)
            if also:
                also(act, 1)
            if gate:
                act.wait_ge(gap_ready, 1)
                nc.scalar.activation(gap[:, :], gap[:, :], ACT.Exp).then_inc(gap_exp, 1)

        @block.tensor
        def _(pe):
            if gate:
                pe.wait_ge(gate_loaded, 32)
            for g in range(G + 1):
                if g < G:
                    pe.wait_ge(xn_ready, g + 1)
                    if g >= 2:
                        pe.wait_ge(xT_sb, 2 * (g - 1))
                    for half in range(2):
                        for t in range(4):
                            last = nc.tensor.transpose(bank[g % 2 * 2 + half][:, t * P:t * P + P],
                                                       xn[g % 2][:, 4 * half + t, :], c["ident"][:, :])
                        last.then_inc(xT_psum, 1)
                if g and gate:
                    pe.wait_ge(xT_sb, 2 * g)
                    for t in range(R):
                        at = ((g - 1) * R + t) * E
                        last = nc.tensor.matmul(bank[4][:, at:at + E], xTc[(g - 1) % 2][:, t * P:t * P + P],
                                                gw[:, :], start=True, stop=True)
                    last.then_inc(logits_done, 1)
            if gate:
                pe.wait_ge(weights_split, 3)
                for t in range(T):
                    if t >= 16 and t % 4 == 0:
                        pe.wait_ge(cT_free, t // 4 - 3)
                    nc.tensor.matmul(bank[t // 4 % 4][0:16, t % 4 * P:t % 4 * P + P], parts[:, t, :],
                                     ident[:, :], start=True, stop=True).then_inc(cT_psum, 1)


def ffn_phase(nc, c, d, name, first, store):
    x, bank = c["x"], c["bank"]
    with ExitStack() as ctx:
        sem = lambda n: ctx.enter_context(nc.semaphore(f"{name}_{n}"))
        sb = lambda n, shape, dt=F32: ctx.enter_context(nc.sbuf_tensor(f"{name}_{n}", shape, dt))
        w1, w1_lo = (sb(n, [P, NE, HID], F32R) for n in ("w1", "w1_lo"))
        w2, w2_lo = (sb(n, [P, NE, HC, D], F32R) for n in ("w2", "w2_lo"))
        b1 = sb("b1", [P, NE * HC])
        b1_rows = sb("b1_rows", [NE * HC, P])
        b2_in = sb("b2_in", [16, D])
        b2 = sb("b2", [16, 2, D], F32R)
        bs2 = sb("bs2", [P, 1])
        xT, xT_lo = (sb(n, [P, T * P], F32R) for n in ("xT", "xT_lo"))
        weightsT = sb("weightsT", [16, T * P], F32R)
        loading = ctx.enter_context(ExitStack())
        w_in = loading.enter_context(nc.sbuf_tensor(f"{name}_w_in", [P, 2, NE, HID], F32))
        weights_loaded, weights_split, act_rounded = map(sem, ("weights_loaded", "weights_split", "act_rounded"))
        N_LOADS = 9

        def loads(sp):
            as_w1, as_w2 = w_in[:, 0, :, :], w_in[:, 1, :, :].rearrange("p e (c d) -> p (e c) d", d=D)
            for dst, src in ((as_w1[:, 0, :], d["ws1"]),
                             (as_w1[:, 1:, :], d["w1"].rearrange("e p h -> p e h")),
                             (as_w2[:, 0:HC, :], d["ws2"].rearrange("(c p) d -> p c d", p=P)),
                             (as_w2[:, HC:, :], d["w2"].rearrange("e (c p) d -> p (e c) d", p=P)),
                             (b1_rows[0:HC, :], d["bs1"].rearrange("(c p) -> c p", p=P)),
                             (b1_rows[HC:, :], d["b1"].rearrange("e (c p) -> (e c) p", p=P)),
                             (b2_in[0:E, :], d["b2"]), (b2_in[E:, :], d["b2"]),
                             (bs2[:, :], d["bs2"].rearrange("(p a) -> p a", a=1))):
                sp.dma_start(dst, src).then_inc(weights_loaded, 16)

        flat2 = lambda w, e: w[:, e, :, :].rearrange("p c d -> p (c d)")
        ROUND_FIRST = 5

        def round_weights(act, part):
            act.wait_ge(weights_loaded, 16 * N_LOADS)
            for e in (range(ROUND_FIRST), range(ROUND_FIRST, NE))[part]:
                for n, high in ((0, w1[:, e, :]), (1, flat2(w2, e))):
                    nc.scalar.activation(high, w_in[:, n, e, :], ACT.Copy).then_inc(act_rounded, 1)

        def split_weights(pool):
            for e in range(NE):
                pool.wait_ge(act_rounded, 2 * e + 2)
                for n, high, low in ((0, w1[:, e, :], w1_lo[:, e, :]), (1, flat2(w2, e), flat2(w2_lo, e))):
                    nc.gpsimd.tensor_tensor(low, w_in[:, n, e, :], high.bitcast(F32), ALU.subtract)\
                        .then_inc(weights_split, 1)

        SPLIT = 2 * NE
        norm_block(nc, c, f"{name}_norm", loads,
                   lambda g, half: (xT[:, bass.ds(g * GT + half * 512, 512)], lambda a: a),
                   low=lambda g: (xT[:, bass.ds(g * GT, GT)], xT_lo[:, bass.ds(g * GT, GT)]),
                   beside=split_weights, also=round_weights, loaded=c["x_loaded"] if first else None,
                   gate={"gate_w": d["gate_w"], "gate_b": d["gate_b"], "weightsT": weightsT})

        loading.close()
        (h_psum, hi_ready, h_ready, lo_ready, down_done, out_free, wide_psum, wide_free, acc_ready, x_psum,
         x_done) = map(sem, ("h_psum", "hi_ready", "h_ready", "lo_ready", "down_done", "out_free", "wide_psum",
                             "wide_free", "acc_ready", "x_psum", "x_done"))
        dve_step, prep_done, b1_psum, passed = map(sem, ("dve_step", "prep_done", "b1_psum", "passed"))
        N_H = 4
        N_HB = 4
        hbank, obank, wbank, tbank = bank[0:3] + bank[7:8], bank[3:5], bank[5], bank[6]
        h = sb("h", [P, N_H, TB])
        h_hi, h_lo = (sb(n, [P, N_H, TB], F32R) for n in ("h_hi", "h_lo"))
        warm = sb("warm", [P, 1])
        acc = sb("acc", [P, TB])
        wide = sb("wide", [P, TB])
        scaled = sb("scaled", [P, TB])
        K = NE * HC
        DOWNS = K + 2
        TURN_AT = 4
        block = ctx.enter_context(nc.Block())

        @block.tensor
        def _(pe):
            pe.wait_ge(weights_split, SPLIT)
            nc.tensor.transpose(bank[7][:, 0:K], b1_rows[:, :], c["ident"][0:K, 0:K]).then_inc(b1_psum, 1)
            pe.wait_ge(prep_done, 3)
            pe.sem_inc(out_free, 2)
            pe.sem_inc(wide_free, 1)

            def turn(done):
                pe.wait_ge(acc_ready, done)
                for t in range(4):
                    last = nc.tensor.transpose(tbank[:, t * P:t * P + P], acc[:, t * P:t * P + P], c["ident"][:, :])
                last.then_inc(x_psum, 1)

            def token_block(tb, first):
                cols = bass.ds(tb * TB, TB)

                def product(out, high, low, in_high, in_low, start, stop, before_low=None):
                    nc.tensor.matmul(out, high, in_high, start=start, stop=False)
                    nc.tensor.matmul(out, low, in_high, start=False, stop=False)
                    if before_low:
                        before_low()
                    return nc.tensor.matmul(out, high, in_low, start=False, stop=stop)

                def up(k):
                    e, part = k // HC, slice(k % HC * P, k % HC * P + P)
                    pe.wait_ge(h_ready, tb * K + k + 1)
                    product(hbank[k % N_HB][:, :], w1[:, e, part], w1_lo[:, e, part], xT[:, cols], xT_lo[:, cols],
                            start=True, stop=True).then_inc(h_psum, 1)

                def down(k):
                    e, chunk = k // HC, k % HC
                    if chunk == 0:
                        if e:
                            wait_alone(pe, wide_free, tb * E + e, passed)
                            nc.tensor.matmul(wbank[:, :], c["sel"][:, e - 1, :], weightsT[:, cols],
                                             start=True, stop=True).then_inc(wide_psum, 1)
                        pe.wait_ge(out_free, tb * NE + e + (1 if e else 2))
                        if e == 0:
                            pe.sem_inc(passed, 1)
                            for part in range(2):
                                nc.tensor.matmul(obank[0][:, :], b2[:, part, :], weightsT[:, cols],
                                                 start=part == 0, stop=False).then_inc(down_done, 1)
                    pe.wait_ge(hi_ready, tb * K + k + 1)
                    product(obank[e % 2][:, :], w2[:, e, chunk, :], w2_lo[:, e, chunk, :], h_hi[:, k % N_H, :],
                            h_lo[:, k % N_H, :], start=chunk == 0 and e > 0, stop=chunk == HC - 1,
                            before_low=lambda: pe.wait_ge(lo_ready, tb * K + k + 1)).then_inc(down_done, 1)

                LEAD = 3
                for k in range(K + LEAD):
                    if k == TURN_AT and not first:
                        turn(tb)
                    if k < K:
                        up(k)
                    if k >= LEAD:
                        down(k - LEAD)

            token_block(0, True)
            with pe.Fori(1, NTB) as tb:
                token_block(tb, False)
            turn(NTB)

        @block.scalar
        def _(act):
            act.sem_inc(down_done, N_H)
            act.sem_inc(h_ready, N_HB)
            act.wait_ge(prep_done, 1)
            nc.scalar.activation(warm[:, :], b1[:, 0:1], ACT.Gelu)
            with act.Fori(0, NTB) as tb:
                for k in range(K):
                    act.wait_ge(h_psum, tb * K + k + 1)
                    act.wait_ge(down_done, tb * DOWNS + (k + 1 if k < N_H else k + 3))
                    for out, ready in ((h_hi, hi_ready), (h, h_ready)):
                        nc.scalar.activation(out[:, k % N_H, :], hbank[k % N_HB][:, :], ACT.Gelu,
                                             bias=b1[:, k:k + 1]).then_inc(ready, 1)

        @block.vector
        def _(dve):
            step = Steps(dve, dve_step)
            dve.wait_ge(b1_psum, 1)
            nc.vector.tensor_copy(b1[:, :], bank[7][:, 0:K]).then_inc(prep_done, 1)
            dve.wait_ge(weights_loaded, 16 * N_LOADS)
            step.did(nc.vector.tensor_copy(b2[:, 0, :], b2_in[:, :]))
            step.wait()
            nc.vector.tensor_tensor(b2[:, 1, :], b2_in[:, :], b2[:, 0, :].bitcast(F32), ALU.subtract).then_inc(prep_done, 1)
            dve.wait_ge(prep_done, 2)
            nc.vector.tensor_copy(scaled[:, 0:1], bs2[:, :]).then_inc(prep_done, 1)
            before = step.n
            PER_TB = E - 1

            def onto_x(done, tb):
                dve.wait_ge(x_psum, done)
                tiles = x[:, :, :].rearrange("p t d -> p (t d)")[:, bass.ds(tb * TB, TB)]
                nc.vector.scalar_tensor_tensor(out=tiles, in0=tbank[:, :], scalar=0.5, in1=tiles,
                                               op0=ALU.mult, op1=ALU.add).then_inc(x_done, 1)

            def token_block(tb, first):
                step.loop(tb * PER_TB + before)

                def low(k):
                    dve.wait_ge(h_ready, tb * K + k + 1 + N_HB)
                    nc.vector.tensor_tensor(h_lo[:, k % N_H, :], h[:, k % N_H, :], h_hi[:, k % N_H, :].bitcast(F32),
                                            ALU.subtract).then_inc(lo_ready, 1)

                def widen(e):
                    dve.wait_ge(wide_psum, tb * E + e)
                    nc.vector.tensor_copy(wide[:, :], wbank[:, :]).then_inc(wide_free, 1)

                def scale(e):
                    dve.wait_ge(down_done, tb * DOWNS + 2 + HC * (e + 1) + N_H)
                    if e:
                        dve.wait_ge(wide_free, tb * E + e + 1)
                        nc.vector.tensor_tensor(scaled[:, :], obank[e % 2][:, :], wide[:, :], ALU.mult)\
                            .then_inc(out_free, 1)
                    else:
                        nc.vector.tensor_scalar(acc[:, :], obank[0][:, :], bs2[:, 0:1], None, ALU.add)\
                            .then_inc(out_free, 1)

                def add(e):
                    dve.wait_ge(out_free, tb * NE + e + 3)
                    if e > 1:
                        step.wait()
                    out = nc.vector.tensor_tensor(acc[:, :], acc[:, :], scaled[:, :], ALU.add)
                    if e < E:
                        step.did(out)
                    else:
                        out.then_inc(acc_ready, 1)

                for k in range(K + HC):
                    if k == TURN_AT and not first:
                        onto_x(tb, tb - 1)
                    if k < K:
                        low(k)
                    e = k // HC - 1
                    if e >= 0 and k % HC == 0 and e:
                        widen(e)
                    if e >= 0 and k % HC == 2:
                        scale(e)
                    if e >= 1 and k % HC == 3:
                        add(e)
                assert step.n == PER_TB

            token_block(0, True)
            with dve.Fori(1, NTB) as tb:
                token_block(tb, False)
            onto_x(NTB, NTB - 1)

        if store:
            @block.sync
            def _(sp):
                for g in range(G):
                    sp.wait_ge(x_done, 2 * g + 2)
                    for j in range(J):
                        sp.dma_start(d["out"][J * g + j].rearrange("(r p) d -> p r d", p=32),
                                     x[32 * j:32 * j + 32, g * R:g * R + R, :]).then_inc(c["stored"], 16)
                sp.wait_ge(c["stored"], 16 * B)


def attention_phase(nc, c, d):
    x = c["x"]
    with ExitStack() as ctx:
        sem = lambda n: ctx.enter_context(nc.semaphore(f"att_{n}"))
        sb = lambda n, shape, dt=F32: ctx.enter_context(nc.sbuf_tensor(f"att_{n}", shape, dt))
        xT = sb("xT", [P, G, J * S])
        w_in = sb("w_in", [P, 2, D])
        w_rep = sb("w_rep", [P, 2, 4, P])
        wv = sb("wv", [P, D])
        wo = sb("wo", [P, D])
        bv = sb("bv", [P, D])
        bo = sb("bo", [P, D])
        w_loaded, w_ready = sem("w_loaded"), sem("w_ready")

        def loads(sp):
            for dst, src in ((w_in[:, 0, :], d["wq"]), (w_in[:, 1, :], d["wk"]), (wv[:, :], d["wv"]),
                             (wo[:, :], d["wo"]), (bv[:, :], d["bv"].partition_broadcast(P)),
                             (bo[:, :], d["bo"].partition_broadcast(P))):
                sp.dma_start(dst, src).then_inc(w_loaded, 16)

        def repeat_weights(pool):
            pool.wait_ge(w_loaded, 16 * 6)
            for n in range(2):
                for copy in range(4):
                    nc.gpsimd.tensor_copy(
                        w_rep[:, n, :, :].rearrange("p q (i c d) -> p (q i) c d", c=4, d=HD)[:, :, copy, :],
                        w_in[:, n, :].rearrange("p (h d) -> p h d", d=HD)).then_inc(w_ready, 1)
            pool.wait_ge(w_ready, 8)

        def xT_view(g, half):
            out = xT[:, :, :].rearrange("p g t -> p (g t)")[:, bass.ds(g * GT, GT)]
            out = out.rearrange("p (j r q) -> p r j q", j=J, q=32)[:, 4 * half:4 * half + 4, :, :]
            return out, lambda a: a.rearrange("p (r j q) -> p r j q", r=4, j=J)

        norm_block(nc, c, "att_norm", loads, xT_view, beside=repeat_weights)

        for general in (False, True):
            heads_block(nc, c, d, xT, w_rep, wv, bv, bo, general)


def heads_block(nc, c, d, xT, w_rep, wv, bv, bo, general):
    x, bank, cols, gain, iw = c["x"], c["bank"], c["cols"], c["gain"], c["iw"]
    with ExitStack() as ctx:
        tag = "gen" if general else "att"
        sem = lambda n: ctx.enter_context(nc.semaphore(f"{tag}_{n}"))
        sb = lambda n, shape, dt=F32: ctx.enter_context(nc.sbuf_tensor(f"{tag}_{n}", shape, dt))
        chosen = lambda eng: eng.If(eng.value_load(c["bounded"][0:1, 0:1]) == (0 if general else 1))
        N_EX = 4
        PAIRS = W // 2
        EARLY = 2
        HQ = H // 4
        xs = sb("xs", [P, J * S])
        wqk = sb("wqk", [P, 2, P])
        wvs = sb("wvs", [P, 4 * HD])
        bqk = sb("bqk", [P, 2])
        bvs = sb("bvs", [P, 4 * HD])
        wos = sb("wos", [4 * HD, D])
        qk = sb("qk", [P, 2, J * S])
        qk_hi = sb("qk_hi", [P, J * S], F32R)
        qs = sb("qs", [P, J * S], F32R)
        ks = sb("ks", [P, J * S], F32R)
        vp = sb("vp", [P, 2 * J, 4, HD])
        vs = sb("vs", [P, 2 * J, 4, HD + 1])
        gm = sb("gm", [P, 2 * J, 4])
        gm_hi = sb("gm_hi", [P, 2 * J, 4], F32R)
        gm_parts = sb("gm_parts", [P, 2 * J, 4, 32])
        gr = sb("gr", [P, J * S], F32R)
        gs = sb("gs", [P, 2, 2 * J, S])
        ex = sb("ex", [P, N_EX, 2 * J, 2, S])
        tr = sb("tr", [P, 2, 4, 16, 32])
        rc = sb("rc", [P, 2, 8, R])
        warm = sb("warm", [P, 1])
        pr = sb("pr", [P, 2, W, R * HD])
        att = sb("att", [P, R, 4 * HD])
        attT = sb("attT", [4 * HD, GT])
        (staged, wo_staged, s_full, s_free, qk_ready, gm_ready, v_ready, gs_ready, ex_ready, av_done, tr_done,
         rc_ready, pr_ready, att_ready, bo_added, dve_step, passed) = map(
            sem, ("staged", "wo_staged", "s_full", "s_free", "qk_ready", "gm_ready", "v_ready", "gs_ready",
                  "ex_ready", "av_done", "tr_done", "rc_ready", "pr_ready", "att_ready", "bo_added", "dve_step",
                  "passed"))
        sbank, abank = bank[0:4], bank[4:8]

        g4 = [("g", n) for n in range(4)]
        v2, p4, r2 = [("v", n) for n in range(2)], [("p", n) for n in range(4)], [("r", n) for n in range(2)]
        m16 = [("m", n) for n in range(16)]
        AHEAD = {
            (0, 0): g4[:2], (0, 1): g4[2:],
            (1, 0): g4[:2], (1, 1): g4[2:],
            (2, 0): g4[:2], (2, 1): g4[2:], (2, 2): v2, (2, 3): p4[:2], (2, 4): p4[2:],
            (2, 5): m16[:4], (2, 6): m16[4:8], (2, 7): m16[8:12],
            (3, 0): m16[12:], (3, 1): r2, (3, 2): g4[:2], (3, 3): g4[2:],
        }
        FIRST = v2 + p4 + m16 + r2 + g4
        if general:
            v2 = [("v", n) for n in range(4)]
            AHEAD = {(0, PAIRS - 1): g4, (1, PAIRS - 1): g4, (2, PAIRS - 1): g4, (3, PAIRS - 1): v2 + p4 + g4}
            FIRST = v2 + p4 + g4
        VM = 2 * J // len(v2)
        CLOSE = 4
        LAP = sum(map(len, AHEAD.values())) + CLOSE
        assert LAP % 4 == 0 and len(FIRST) % 4 == 0
        START = LAP - len(FIRST)

        STAGES = 6
        HEADS_STEPS = 7 if general else 12
        if general:
            score, turns, angle, largest = (ex[:, n // 2, J * (n % 2):J * (n % 2) + J, :, :]
                                            .rearrange("p a b q -> p (a b q)") for n in range(2, 6))
            total, part = sb("total", [P, R, HD]), sb("part", [P, R, HD])
            channel_step, angle_ready, sin_ready, f_ready, largest_ready, less_ready = map(
                sem, ("channel_step", "angle_ready", "sin_ready", "f_ready", "largest_ready", "less_ready"))
            CHANNEL_STEPS = 15

        def channel_general(dve, channel, column, w, i):
            step = Steps(dve, channel_step)
            step.loop(channel * CHANNEL_STEPS)

            def then(instruction):
                step.did(instruction)
                step.wait()

            v = nc.vector
            then(v.tensor_scalar(score, gs[:, i % 2, :, :].rearrange("p a q -> p (a q)"),
                                 gain[:, bass.ds(column, 1)], None, ALU.mult))
            then(v.scalar_tensor_tensor(out=angle, in0=score, scalar=KERR, in1=score, op0=ALU.mult, op1=ALU.mult))
            then(v.tensor_scalar(turns, angle, float(1 / (2 * np.pi)), MAGIC, ALU.mult, ALU.add))
            then(v.tensor_scalar(turns, turns, -MAGIC, None, ALU.add))
            for turn_part in (TWO_PI_A, TWO_PI_B, TWO_PI_C):
                then(v.scalar_tensor_tensor(out=angle, in0=turns, scalar=-turn_part, in1=angle,
                                            op0=ALU.mult, op1=ALU.add))
            v.tensor_scalar(turns, angle, PI_BELOW, -PI_BELOW, ALU.min, ALU.max).then_inc(angle_ready, 1)
            dve.wait_ge(sin_ready, channel + 1)
            then(v.tensor_tensor(turns, turns, turns, ALU.mult))
            then(v.tensor_scalar(turns, turns, -2.0, 1.0, ALU.mult, ALU.add))
            v.tensor_tensor(score, score, turns, ALU.mult).then_inc(f_ready, 1)
            dve.wait_ge(largest_ready, channel + 1)
            top = largest.rearrange("p (j a q) -> p j a q", a=2, q=S)
            then(v.tensor_tensor(top[:, :, 0, :], top[:, :, 0, :], top[:, :, 1, :], ALU.max))
            by_half = score.rearrange("p (j a q) -> p j a q", a=2, q=S)
            for a in range(2):
                v.tensor_tensor(by_half[:, :, a, :], by_half[:, :, a, :], top[:, :, 0, :], ALU.subtract)\
                    .then_inc(less_ready, 1)
            dve.wait_ge(av_done, channel + (1 + N_EX))
            out = tr[:, 0, 0, 0:R, :]
            then(v.transpose(out.rearrange("p r c -> p (r c)"), abank[0][:, 0:S]))
            then(v.reciprocal(rc[:, 0, 0, :], out[:, :, HD]))
            then(v.tensor_scalar(rc[:, 0, 0, :], rc[:, 0, 0, :], iw[:, bass.ds(w, 1)], None, ALU.mult))
            then(v.tensor_tensor(part[:, :, :], out[:, :, 0:HD],
                                 rc[:, 0, 0, :].unsqueeze(2).to_broadcast([P, R, HD]), ALU.mult))
            then(v.tensor_tensor(total[:, :, :], total[:, :, :], part[:, :, :], ALU.add))
            assert step.n == CHANNEL_STEPS, step.n

        def reduce_unit(dve, it, i):
            dve.wait_ge(pr_ready, (it * 4 + i) * 2 + 4)
            nc.vector.reduce_sum(att[:, :, i * HD:i * HD + HD],
                                 pr[:, i % 2, :, :].rearrange("p w (r d) -> p r d w", d=HD), axis=AX)\
                .then_inc(att_ready, 1)

        block = ctx.enter_context(nc.Block())

        @block.sync
        def _(sp):
            with chosen(sp):
                def stage(g, hq):
                    sp.dma_start(xs[:, :], xT[:, :, :].rearrange("p g t -> p (g t)")[:, bass.ds(g * GT, GT)])\
                        .then_inc(staged, 16)
                    for n in range(2):
                        sp.dma_start(wqk[:, n, :], w_rep[:, n, :, :].rearrange("p q c -> p (q c)")[:, bass.ds(hq * P, P)])\
                            .then_inc(staged, 16)
                    sp.dma_start(wvs[:, :], wv[:, bass.ds(hq * 32, 32)]).then_inc(staged, 16)
                    sp.dma_start(bvs[:, :], bv[:, bass.ds(hq * 32, 32)]).then_inc(staged, 16)
                    sp.dma_start(bqk[:, :], cols[:, bass.ds(hq * 2, 2)]).then_inc(staged, 16)

                sp.sem_inc(qk_ready, 1)
                with sp.Fori(0, G) as g:
                    with sp.Fori(0, HQ) as hq:
                        sp.wait_ge(qk_ready, g * HQ + hq + 1)
                        stage(g, hq)
                sp.wait_ge(qk_ready, G * HQ + 1)
                stage(G - 1, HQ - 1)
                sp.wait_ge(staged, STAGES * 16 * (G * HQ + 1))

        @block.tensor
        def _(pe):
            with chosen(pe):
                def fill(kind, n, index, lap, i_next, it_next):
                    out = sbank[index % 4]
                    use = lap + index
                    pe.wait_ge(s_free, use + 1)
                    rows = slice(32 * i_next, 32 * i_next + 32)
                    if kind == "v":
                        if n == 0:
                            pe.wait_ge(staged, (it_next + 1) * (16 * STAGES))
                        for m in range(VM):
                            last = nc.tensor.matmul(out[:, m * 32:m * 32 + 32],
                                                    xs[:, (VM * n + m) * P:(VM * n + m + 1) * P], wvs[:, :],
                                                    start=True, stop=True)
                    elif kind == "p":
                        last = nc.tensor.matmul(out[:, :], wqk[:, n // 2, :], xs[:, n % 2 * 512:n % 2 * 512 + 512],
                                                start=True, stop=True)
                    elif kind == "m":
                        if n == 0:
                            pe.wait_ge(qk_ready, it_next + 2)
                        j, rows = n // 4, slice(32 * (n % 4), 32 * (n % 4) + 32)
                        for half in range(2):
                            at = j * S + half * P
                            last = nc.tensor.matmul(out[:, half * S:half * S + S], qs[rows, at:at + P],
                                                    ks[rows, j * S:j * S + S], start=True, stop=True)
                    elif kind == "r":
                        if n == 0:
                            pe.wait_ge(gm_ready, 2 * it_next + 2)
                        for m in range(4):
                            last = nc.tensor.matmul(out[:, m * P:m * P + P],
                                                    gm_parts[:, 4 * n + m, :, :].rearrange("p a b -> p (a b)"),
                                                    c["ident"][:, :], start=True, stop=True)
                    elif kind == "g":
                        if n == 0 and i_next == 0 and general:
                            pe.wait_ge(qk_ready, it_next + 2)
                        elif n == 0 and i_next == 0:
                            pe.wait_ge(s_free, use + 4)
                        for half in range(2):
                            at = n * S + half * P
                            last = nc.tensor.matmul(out[:, half * S:half * S + S], ks[rows, at:at + P],
                                                    qs[rows, n * S:n * S + S], start=True, stop=general)
                            if not general:
                                two = slice(rows.start, rows.start + 2)
                                last = nc.tensor.matmul(out[:, half * S:half * S + S], c["minus"][two, :],
                                                        gr[two, n * S:n * S + S], start=False, stop=True)
                    elif kind == "turn":
                        if n == 0:
                            pe.wait_ge(att_ready, it_next * 4 + 2)
                        for t in range(4):
                            last = nc.tensor.transpose(out[0:32, t * P:t * P + P], att[:, 4 * n + t, :], c["ident"][:, :])
                    else:
                        if n == 0:
                            pe.wait_ge(wo_staged, it_next * 16)
                        pe.wait_ge(s_free, use + 3)
                        for t in range(4):
                            last = nc.tensor.matmul(out[:, t * P:t * P + P], attT[:, (4 * n + t) * P:(4 * n + t) * P + P],
                                                    wos[:, :], start=True, stop=True)
                    last.then_inc(s_full, 1)

                for index, (kind, n) in enumerate(FIRST):
                    fill(kind, n, START + index, 0, 0, 0)

                def pair_products(it, i, p):
                    pair = it * (4 * PAIRS) + (i * PAIRS + p)
                    pe.wait_ge(ex_ready, pair * 2 + (2 + 2 * W))
                    pe.wait_ge(tr_done, pair + 1)
                    for half in range(2):
                        for j in range(J):
                            last = nc.tensor.matmul(
                                abank[p % 4][32 * j:32 * j + HD + 1, :], vs[:, 2 * j + half, i, :],
                                ex[:, p % N_EX, 2 * j + half, :, :].rearrange("p a b -> p (a b)"),
                                start=half == 0, stop=half == 1)
                    last.then_inc(av_done, 1)

                def channel_products(it, i):
                    with pe.Fori(0, W) as w:
                        channel = (it * 4 + i) * W + w
                        pe.wait_ge(ex_ready, channel + (1 + 2 * W))
                        for half in range(2):
                            for j in range(J):
                                last = nc.tensor.matmul(
                                    abank[0][32 * j:32 * j + HD + 1, 0:S], vs[:, 2 * j + half, i, :],
                                    ex[:, 0, 2 * j + half, 0, :], start=half == 0, stop=half == 1)
                        last.then_inc(av_done, 1)

                def begin(it):
                    wait_alone(pe, v_ready, it + 1, passed)
                    for p in range(0 if general else EARLY):
                        pair_products(it, 0, p)

                def head_group(it, is_last):
                    lap = (it + 1) * LAP
                    index = 0
                    for i in range(4):
                        if general:
                            channel_products(it, i)
                        for p in range(PAIRS):
                            if not general and (i or p >= EARLY):
                                pair_products(it, i, p)
                            for kind, n in AHEAD.get((i, p), ()):
                                fill(kind, n, index, lap, (i + 1) % 4, it + 1)
                                index += 1
                    if not is_last:
                        begin(it + 1)
                    for kind, n in (("turn", 0), ("turn", 1), ("out", 0), ("out", 1)):
                        fill(kind, n, index, lap, 0, it + 1)
                        index += 1

                begin(0)
                with pe.Fori(0, G * HQ - 1) as it:
                    head_group(it, False)
                head_group(G * HQ - 1, True)

        @block.scalar
        def _(act):
            with chosen(act):
                act.sem_inc(av_done, N_EX)
                act.sem_inc(ex_ready, 2 * W)
                channel_gain = [act.alloc_register(f"{tag}_gain{n}") for n in range(4)]
                nc.scalar.activation(warm[:, :], iw[:, 0:1], ACT.Exp)
                with act.Fori(0, G) as g:
                    with act.Fori(0, HQ) as hq:
                        it = g * HQ + hq
                        for i in range(4):
                            if general:
                                with act.Fori(0, W) as w:
                                    channel = (it * 4 + i) * W + w
                                    act.wait_ge(angle_ready, channel + 1)
                                    nc.scalar.activation(turns[:, :], turns[:, :], ACT.Sin, scale=0.5)\
                                        .then_inc(sin_ready, 1)
                                    act.wait_ge(less_ready, channel * 2 + 2)
                                    nc.scalar.activation(ex[:, 0, :, 0, :], score[:, :].rearrange("p (a q) -> p a q", q=S),
                                                         ACT.Exp).then_inc(ex_ready, 1)
                                continue
                            for w in range(W):
                                act.reg_load(channel_gain[w % 4], gain[0:1, bass.ds(hq * (4 * W) + (i * W + w), 1)]
                                             .bitcast(mybir.dt.int32))
                                if w == 0:
                                    act.wait_ge(gs_ready, it * 4 + i + 1)
                                if w % 2 == 0:
                                    act.wait_ge(av_done, it * (4 * PAIRS) + (i * PAIRS + w // 2 + 1))
                                nc.scalar.activation(ex[:, w // 2 % N_EX, :, w % 2, :], gs[:, i % 2, :, :], ACT.Exp,
                                                     scale=channel_gain[w % 4])\
                                    .then_inc(ex_ready, 1)

        @block.vector
        def _(dve):
            with chosen(dve):
                step = Steps(dve, dve_step)
                dve.sem_inc(s_free, START + 4)
                dve.sem_inc(s_full, START)
                dve.sem_inc(tr_done, 4)
                for b in abank:
                    step.did(nc.vector.memset(b[:, :], 0.0))
                step.did(nc.vector.memset(vs[:, :, :, :], 1.0))
                step.did(nc.vector.memset(gm_parts[:, :, :, :], 0.0))
                step.wait()
                before = step.n

                def split(n, last):
                    step.did(nc.vector.tensor_copy(qk_hi[:, :], qk[:, n, :]))
                    step.wait()
                    out = nc.vector.scalar_tensor_tensor(
                        out=(qs, ks)[n][:, :], in0=qk_hi[:, :].bitcast(F32), scalar=cols[:, 8 + n:9 + n],
                        in1=qk[:, n, :], op0=ALU.mult, op1=ALU.add)
                    if last:
                        out.then_inc(qk_ready, 1)
                    else:
                        step.did(out)

                def empty(kind, n, index, lap, i_next, it_next, g=None):
                    src = sbank[index % 4]
                    use = lap + index
                    dve.wait_ge(s_full, use + 1)
                    if kind == "v":
                        if n == 0:
                            dve.wait_ge(staged, (it_next + 1) * (16 * STAGES))
                        nc.vector.tensor_tensor(
                            vp[:, VM * n:VM * n + VM, :, :].rearrange("p m i d -> p m (i d)"),
                            src[:, 0:VM * 32].rearrange("p (m n) -> p m n", m=VM),
                            bvs[:, :].unsqueeze(1).to_broadcast([P, VM, 4 * HD]), ALU.add).then_inc(s_free, 1)
                    elif kind == "p":
                        nc.vector.tensor_scalar(qk[:, n // 2, n % 2 * 512:n % 2 * 512 + 512], src[:, :],
                                                bqk[:, n // 2:n // 2 + 1], None, ALU.add).then_inc(s_free, 1)
                        if n % 2 == 1:
                            dve.wait_ge(s_free, use + 5)
                            split(n // 2, n == 3)
                    elif kind == "m":
                        nc.vector.reduce_max(gm[:, 2 * (n // 4):2 * (n // 4) + 2, n % 4],
                                             src[:, :].rearrange("p (a k) -> p a k", a=2), axis=AX).then_inc(s_free, 1)
                        if n == 15:
                            dve.wait_ge(s_free, use + 5)
                            step.did(nc.vector.tensor_copy(gm_hi[:, :, :], gm[:, :, :]))
                            step.wait()
                            nc.vector.tensor_copy(gm_parts[:, :, :, 0], gm_hi[:, :, :].bitcast(F32)).then_inc(gm_ready, 1)
                            nc.vector.tensor_tensor(gm_parts[:, :, :, 1], gm[:, :, :], gm_hi[:, :, :].bitcast(F32),
                                                    ALU.subtract).then_inc(gm_ready, 1)
                    elif kind == "r":
                        nc.vector.tensor_copy(gr[:, n * 512:n * 512 + 512], src[:, :]).then_inc(s_free, 1)
                    elif kind == "g":
                        nc.vector.tensor_copy(gs[:, i_next % 2, 2 * n:2 * n + 2, :].rearrange("p a q -> p (a q)"),
                                              src[:, :]).then_inc(s_free, 1)
                        if n == 3:
                            dve.drain().then_inc(gs_ready, 1)
                    elif kind == "turn":
                        nc.vector.tensor_copy(attT[:, n * 512:n * 512 + 512], src[0:32, :]).then_inc(s_free, 1)
                    else:
                        tiles = x[:, :, :].rearrange("p t d -> p (t d)")[:, bass.ds(g * GT + n * 512, 512)]
                        nc.vector.tensor_tensor(tiles, src[:, :], tiles, ALU.add).then_inc(s_free, 1)

                for index, (kind, n) in enumerate(FIRST):
                    empty(kind, n, START + index, 0, 0, 0)
                first_steps = step.n
                nc.vector.tensor_copy(vs[:, :, :, 0:HD], vp[:, :, :, :]).then_inc(v_ready, 1)
                dve.wait_ge(bo_added, 1)

                with dve.Fori(0, G) as g:
                    with dve.Fori(0, HQ) as hq:
                        it = g * HQ + hq
                        step.loop(it * HEADS_STEPS + first_steps)
                        lap = (it + 1) * LAP
                        index = 0
                        for i in range(4):
                            if general:
                                dve.wait_ge(gs_ready, it * 4 + (i + 1))
                                step.did(nc.vector.memset(total[:, :, :], 0.0))
                                wait_alone(dve, dve_step, step.base + step.n, passed)
                                with dve.Fori(0, W) as w:
                                    channel = (it * 4 + i) * W + w
                                    channel_general(dve, channel, hq * (4 * W) + i * W + w, w, i)
                                nc.vector.tensor_copy(att[:, :, i * HD:i * HD + HD], total[:, :, :]).then_inc(att_ready, 1)
                                for kind, n in AHEAD[i, PAIRS - 1]:
                                    empty(kind, n, index, lap, (i + 1) % 4, it + 1)
                                    index += 1
                                continue
                            for p in range(PAIRS):
                                pair = it * (4 * PAIRS) + (i * PAIRS + p)
                                half, unit = p // 4, it * 4 + i
                                if p % 4 == 0:
                                    dve.wait_ge(pr_ready, unit * 2 + (half + 1))
                                dve.wait_ge(av_done, pair + (1 + N_EX))
                                nc.vector.transpose(tr[:, half, p % 4, :, :].rearrange("p a b -> p (a b)"),
                                                    abank[p % 4][:, :]).then_inc(tr_done, 1)
                                if p % 4 == 3:
                                    dve.wait_ge(tr_done, pair + 5)
                                    step.did(nc.vector.reciprocal(
                                        rc[:, half, :, :].rearrange("p w r -> p (w r)"),
                                        tr[:, half, :, :, :].rearrange("p a b c -> p (a b) c")[:, :, HD]))
                                    step.wait()
                                    nc.vector.tensor_tensor(rc[:, half, :, :], rc[:, half, :, :],
                                                            iw[:, 8 * half:8 * half + 8].unsqueeze(2)
                                                            .to_broadcast([P, 8, R]), ALU.mult).then_inc(rc_ready, 1)
                                if i and p == 1:
                                    reduce_unit(dve, it, i - 1)
                                for kind, n in AHEAD.get((i, p), ()):
                                    if kind == "g" and n == 0:
                                        dve.wait_ge(ex_ready, unit * W + 2 * W)
                                    empty(kind, n, index, lap, (i + 1) % 4, it + 1)
                                    index += 1
                        dve.wait_ge(av_done, (it + 1) * (4 * (W if general else PAIRS)) + N_EX)
                        nc.vector.tensor_copy(vs[:, :, :, 0:HD], vp[:, :, :, :]).then_inc(v_ready, 1)
                        if not general:
                            reduce_unit(dve, it, 3)
                        for kind, n in (("turn", 0), ("turn", 1), ("out", 0), ("out", 1)):
                            empty(kind, n, index, lap, 0, it + 1, g)
                            index += 1
                        assert step.n == HEADS_STEPS, step.n

        @block.gpsimd
        def _(pool):
            with chosen(pool):
                pool.sem_inc(pr_ready, 2)
                pool.sem_inc(att_ready, 2)
                xall = x[:, :, :]
                nc.gpsimd.tensor_tensor(xall, xall, bo[:, :].unsqueeze(1).to_broadcast([P, T, D]), ALU.add)\
                    .then_inc(bo_added, 1)
                with pool.Fori(0, G) as g:
                    with pool.Fori(0, HQ) as hq:
                        it = g * HQ + hq
                        pool.wait_ge(s_free, it * LAP + (LAP + 4))
                        pool.dma_start(wos[:, :], d["wo"][bass.ds(hq * 32, 32), :]).then_inc(wo_staged, 16)
                        for i in range(4):
                            unit = it * 4 + i
                            if general:
                                with pool.Fori(0, W) as w:
                                    channel = unit * W + w
                                    wait_alone(pool, f_ready, channel + 1, passed)
                                    nc.gpsimd.partition_all_reduce(largest, score, P, bass.bass_isa.ReduceOp.max)\
                                        .then_inc(largest_ready, 1)
                                continue
                            for half in range(2):
                                pool.wait_ge(rc_ready, unit * 2 + (half + 1))
                                if half == 0:
                                    pool.wait_ge(att_ready, unit + 1)
                                nc.gpsimd.tensor_tensor(
                                    pr[:, i % 2, 8 * half:8 * half + 8, :].rearrange("p w (r d) -> p (w r) d", d=HD),
                                    tr[:, half, :, :, :].rearrange("p a b c -> p (a b) c")[:, :, 0:HD],
                                    rc[:, half, :, :].rearrange("p w r -> p (w r)").unsqueeze(2)
                                    .to_broadcast([P, 8 * R, HD]), ALU.mult).then_inc(pr_ready, 1)
                pool.wait_ge(wo_staged, 16 * G * HQ)


def macaron_kernel(nc, d):
    with ExitStack() as ctx:
        sb = lambda n, shape, dt=F32: ctx.enter_context(nc.sbuf_tensor(n, shape, dt))
        c = {
            "x": sb("x", [P, T, D]),
            "ident": sb("ident", [P, P]),
            "iota": sb("iota", [P, E], mybir.dt.int32),
            "iotaf": sb("iotaf", [P, E]),
            "sel": sb("sel_r", [16, E, P], F32R),
            "minus": sb("minus", [P, P], F32R),
            "iw": sb("iw", [P, W]),
            "gain": sb("gain", [P, H * W]),
            "bounded": sb("bounded", [1, 1], mybir.dt.int32),
            "cols": sb("cols", [P, 10]),
            "bank": [ctx.enter_context(nc.psum_tensor(f"bank{n}", [P, 512], F32)) for n in range(8)],
            "x_loaded": ctx.enter_context(nc.semaphore("x_loaded")),
            "stored": ctx.enter_context(nc.semaphore("stored")),
        }
        setup_block(nc, c, d)
        ffn_phase(nc, c, d, "ffn1", first=True, store=False)
        attention_phase(nc, c, d)
        ffn_phase(nc, c, d, "ffn2", first=False, store=True)


_NAMES = {
    "x": "L0_attn_x", "wq": "L0_attn_Wq", "bq": "L0_attn_bq", "wk": "L0_attn_Wk", "bk": "L0_attn_bk",
    "wv": "L0_attn_Wv", "bv": "L0_attn_bv", "wo": "L0_attn_Wo", "bo": "L0_attn_bo",
    "pm": "L0_attn_phase_modulators", "iw": "L0_attn_interference_weights",
    "gate_w": "L0_ffn_gate_w", "gate_b": "L0_ffn_gate_b", "w1": "L0_ffn_w1", "b1": "L0_ffn_b1",
    "w2": "L0_ffn_w2", "b2": "L0_ffn_b2", "ws1": "L0_ffn_ws1", "bs1": "L0_ffn_bs1",
    "ws2": "L0_ffn_ws2", "bs2": "L0_ffn_bs2",
}


def kernel(**inputs):
    import concourse.bacc as bacc
    from concourse.bass_utils import run_bass_kernel_spmd

    nc = bacc.Bacc("TRN2", target_bir_lowering=False, num_devices=1)
    arrays, d = {}, {}
    for short, name in _NAMES.items():
        a = np.ascontiguousarray(inputs[name])
        arrays[name] = a
        d[short] = nc.dram_tensor(name, a.shape, mybir.dt.from_np(a.dtype), kind="ExternalInput").ap()
    d["out"] = nc.dram_tensor("out", (B, S, D), F32, kind="ExternalOutput").ap()
    macaron_kernel(nc, d)
    return run_bass_kernel_spmd(nc, [arrays], core_ids=[0]).results[0]["out"]
```
